# Optimizing a Trainium2 kernel written in Bass

```python
import numpy as np
import jax
import jax.numpy as jnp

def _softmax(x, axis=-1):
    return jax.nn.softmax(x, axis=axis)

def _gelu(x):
    return jax.nn.gelu(x, approximate=True)

def _silu(x):
    return jax.nn.silu(x)

def _sigmoid(x):
    return jax.nn.sigmoid(x)

def _layernorm(x, axis=-1, eps=1e-05):
    m = jnp.mean(x, axis=axis, keepdims=True)
    v = jnp.var(x, axis=axis, keepdims=True)
    return (x - m) / jnp.sqrt(v + eps)

def _scatter_add(tgt, idx, src, axis=0):
    return tgt.at[idx].add(src)

def _segment_sum(src, seg, n):
    return jax.ops.segment_sum(src, seg, n)
kernel_name = 'mk_sandwich_d1_jaxref_r4_0dc602'

def setup_inputs(seed: int=0):
    np.random.seed(seed)
    _w = jnp.asarray

    def _L0_attn_setup():
        import jax, jax.numpy as jnp
        import numpy as np
        D_MODEL = 256
        NUM_HEADS = 16
        D_K = D_MODEL // NUM_HEADS
        B, S = (4, 512)
        key = jax.random.key(seed)
        k1, k2, k3 = jax.random.split(key, 3)
        x = jax.random.normal(k1, (B, S, D_MODEL), dtype=jnp.float32)
        w_qkv = jax.random.normal(k2, (3, NUM_HEADS, D_K, D_MODEL), dtype=jnp.float32) / np.sqrt(D_MODEL)
        w_o = jax.random.normal(k3, (D_MODEL, D_MODEL), dtype=jnp.float32) / np.sqrt(D_MODEL)
        return {'x': x, 'w_qkv': w_qkv, 'w_o': w_o}
    _L0_attn_in = _L0_attn_setup()

    def _L0_ffn_setup():
        import jax, jax.numpy as jnp
        import numpy as np
        D_MODEL, D_FF, RANK = (256, 1024, 64)
        B, S = (4, 1024)
        key = jax.random.key(seed)
        ks = jax.random.split(key, 7)
        return {'x': jax.random.normal(ks[0], (B, S, D_MODEL), dtype=jnp.float32), 'U1': jax.random.normal(ks[1], (D_MODEL, RANK), dtype=jnp.float32) * 0.02, 'V1': jax.random.normal(ks[2], (RANK, D_FF), dtype=jnp.float32) * 0.02, 'b1': jnp.zeros((D_FF,), dtype=jnp.float32), 'U2': jax.random.normal(ks[3], (D_FF, RANK), dtype=jnp.float32) * 0.02, 'V2': jax.random.normal(ks[4], (RANK, D_MODEL), dtype=jnp.float32) * 0.02, 'b2': jnp.zeros((D_MODEL,), dtype=jnp.float32)}
    _L0_ffn_in = _L0_ffn_setup()
    _d = {'L0_attn_x': _L0_attn_in['x'], 'L0_attn_w_qkv': _L0_attn_in['w_qkv'], 'L0_attn_w_o': _L0_attn_in['w_o'], 'L0_ffn_U1': _L0_ffn_in['U1'], 'L0_ffn_V1': _L0_ffn_in['V1'], 'L0_ffn_b1': _L0_ffn_in['b1'], 'L0_ffn_U2': _L0_ffn_in['U2'], 'L0_ffn_V2': _L0_ffn_in['V2'], 'L0_ffn_b2': _L0_ffn_in['b2']}
    _x0 = _d['L0_attn_x']
    _d['L0_attn_x'] = jax.random.normal(jax.random.fold_in(jax.random.key(seed), 1), (8, 1024, 256), dtype=_x0.dtype)
    del _x0
    return _d

def reference(L0_attn_x, L0_attn_w_qkv, L0_attn_w_o, L0_ffn_U1, L0_ffn_V1, L0_ffn_b1, L0_ffn_U2, L0_ffn_V2, L0_ffn_b2):

    def _L0_attn_ref(x, w_qkv, w_o):
        import jax, jax.numpy as jnp
        import numpy as np
        D_MODEL = 256
        NUM_HEADS = 16
        D_K = D_MODEL // NUM_HEADS
        B, S = (4, 512)
        seq_len = x.shape[-2]
        d_k = w_qkv.shape[-2]
        qkv = jnp.einsum('bsm,qhkm->qbhsk', x, w_qkv)
        Q, K, V = (qkv[0], qkv[1], qkv[2])
        scores = jnp.einsum('bhsk,bhtk->bhst', Q, K) / jnp.sqrt(jnp.asarray(d_k, x.dtype))
        causal = jnp.tril(jnp.ones((seq_len, seq_len), dtype=bool))
        scores = jnp.where(causal, scores, -jnp.inf)
        probs = jax.nn.softmax(scores, axis=-1)
        attn = jnp.einsum('bhst,bhtk->bhsk', probs, V)
        b, h, s, k = attn.shape
        attn_cat = jnp.transpose(attn, (0, 2, 1, 3)).reshape(b, s, h * k)
        return jnp.einsum('bsd,md->bsm', attn_cat, w_o)

    def _L0_ffn_ref(x, U1, V1, b1, U2, V2, b2):
        import jax, jax.numpy as jnp
        import numpy as np
        D_MODEL, D_FF, RANK = (256, 1024, 64)
        B, S = (4, 1024)
        P = jnp.einsum('bsd,dr->bsr', x, U1)
        H = jax.nn.gelu(jnp.einsum('bsr,rf->bsf', P, V1) + b1)
        Q = jnp.einsum('bsf,fr->bsr', H, U2)
        return jnp.einsum('bsr,rd->bsd', Q, V2) + b2
    x = L0_attn_x
    x = x + _layernorm(_L0_attn_ref(_layernorm(x, axis=-1), L0_attn_w_qkv, L0_attn_w_o), axis=-1)
    x = x + _layernorm(_L0_ffn_ref(_layernorm(x, axis=-1), L0_ffn_U1, L0_ffn_V1, L0_ffn_b1, L0_ffn_U2, L0_ffn_V2, L0_ffn_b2), axis=-1)
    return x

_drawn_inputs = setup_inputs


def setup_inputs(seed=0):
    import zlib

    import numpy as np

    out = dict(_drawn_inputs(seed))
    spreads = {'L0_ffn_b1': (0.0, 0.1), 'L0_ffn_b2': (0.0, 0.1)}
    factors = {'L0_ffn_U1': 3.59, 'L0_ffn_V1': 3.605}
    for name, (base, spread) in spreads.items():
        noise = np.random.default_rng([zlib.crc32(name.encode()), seed]).standard_normal(out[name].shape)
        drawn = base * np.exp(spread * noise) if base else spread * noise
        out[name] = jnp.asarray(drawn.astype(out[name].dtype))
    for name, factor in factors.items():
        out[name] = (out[name] * factor).astype(out[name].dtype)
    return out
```

```python
from contextlib import ExitStack

import concourse.bass as bass
from concourse import mybir

F32 = mybir.dt.float32
F32R = mybir.dt.float32r
BF16 = mybir.dt.bfloat16
ALU = mybir.AluOpType
ACT = mybir.ActivationFunctionType

P = 128
DK = 16
QUAD = 4
CH = 512
EPS = 1e-5
NEG = -3.0e38
STACK = 3 * DK
RING = 3


def build(nc, x, w_qkv_t, w_o_t, u1, v1, b1_t, u2, v2, b2, ident_in, out):
    B, S, D = x.shape
    H = D // DK
    RANK = u1.shape[1]
    FF = v1.shape[1]
    NT = S // P
    NC = S // CH
    TC = CH // P
    KD = D // P
    NF = FF // P
    NQ = H // QUAD
    HT = P // DK
    VW = DK + 1

    STEPS = [(c, kt) for c in range(NC) for kt in range(TC * (c + 1))]
    NS = len(STEPS)
    TOTAL = NQ * NS

    def width(k):
        c, kt = STEPS[k]
        first = max(c * CH, kt * P)
        return first, (c + 1) * CH - first

    def diagonal(k):
        c, kt = STEPS[k]
        return kt >= TC * c

    def diagonals(s):
        return sum(diagonal(t % NS) for t in range(s))

    UNITS = [(i, j) for i in range(NT) for j in range(QUAD)]
    SPREAD = 9
    _cols = [width(k)[1] for k in range(SPREAD)]
    _all = sum(i + 1 for i, j in UNITS)
    UNITS_AT, _n, _done = [], 0, 0
    for k in range(SPREAD):
        goal = _all * sum(_cols[:k + 1]) / sum(_cols)
        here = []
        while _n < len(UNITS) and (_done < goal - 0.5 or k == SPREAD - 1):
            here.append(UNITS[_n])
            _done += UNITS[_n][0] + 1
            _n += 1
        UNITS_AT.append(here)
    UNITS_AT += [[] for _ in range(NS - SPREAD)]
    NU = len(UNITS)

    ctx = ExitStack()

    def sb(name, shape, dt=F32):
        return ctx.enter_context(nc.sbuf_tensor(name, shape, dt))

    sems = []

    def sem(name):
        s = ctx.enter_context(nc.semaphore(name))
        sems.append(s)
        return s

    with ctx:
        wqkv = sb("wqkv", [P, KD, 3 * D])
        wo = sb("wo", [P, KD, D])
        u1s = sb("u1s", [P, KD, RANK])
        v1s = sb("v1s", [RANK, FF])
        b1s = sb("b1s", [P, NF])
        u2s = sb("u2s", [P, NF, RANK])
        v2s = sb("v2s", [2 * RANK, D])
        b2s = sb("b2s", [P, D])
        ident = sb("ident", [P, P])
        mask = sb("mask", [P, S], BF16)
        mhalf = sb("mhalf", [P, NT])
        xin = sb("xin", [P, NT, D])
        xnT = sb("xnT", [P, KD, S])
        parts = sb("parts", [P, 2, 2, S], F32R)
        qst = sb("qst", [P, NQ, 2, S], F32R)
        kst = sb("kst", [P, NQ, 2, S], F32R)
        vaug = sb("vaug", [P, NT, H * VW + DK])
        prob = sb("prob", [P, RING, QUAD, CH])
        rmax = sb("rmax", [P, QUAD * NT])
        mrow = sb("mrow", [QUAD * NT, 2, P], F32R)
        oacc = sb("oacc", [P, 2, CH])
        rden = sb("rden", [P, TC, QUAD])
        att = sb("att", [P, NT, D])
        xres = sb("xres", [P, NT, D])
        y = sb("y", [P, NT, D])
        x2T = sb("x2T", [P, KD, CH])
        lowT = sb("lowT", [RANK, CH])
        hid = sb("hid", [P, NF, CH])
        attT = hid[:, :, :].rearrange("p f n -> p (f n)")[:, 0:KD * S].rearrange("p (k n) -> p k n", k=KD)
        backT = sb("backT", [2 * RANK, CH])
        bst = sb("bst", [P, 4, TC, 6])
        mv = sb("mv", [P, 4, TC, 2])
        rstd = sb("rstd", [P, 4, TC])

        ps_max = ctx.enter_context(nc.psum_tensor("ps_max", [P, 2, S], F32))
        ps_st = ctx.enter_context(nc.psum_tensor("ps_st", [P, 2, CH], F32))
        ps_pv = ctx.enter_context(nc.psum_tensor("ps_pv", [P, CH], F32))
        ps_side = ctx.enter_context(nc.psum_tensor("ps_side", [P, CH], F32))

        w_loaded = sem("w_loaded")
        consts_set = sem("consts_set")
        xin_loaded = [sem(f"xin_loaded{c}") for c in range(NC)]
        xres_loaded = sem("xres_loaded")
        max_full = sem("max_full")
        max_read = sem("max_read")
        st_full = sem("st_full")
        exp_done = sem("exp_done")
        masked = sem("masked")
        pv_done = sem("pv_done")
        acc_read = sem("acc_read")
        side_full = sem("side_full")
        side_free = sem("side_free")
        high_done = sem("high_done")
        gelu_done = sem("gelu_done")
        stats_done = [sem(f"stats_done{n}") for n in range(4)]
        norm_done = [sem(f"norm_done{n}") for n in range(4)]
        dve_step = sem("dve_step")
        pool_step = sem("pool_step")
        stacked = [sem(f"stacked{g}") for g in range(NQ)]
        mrow_set = sem("mrow_set")
        stored = sem("stored")

        x_b = x.rearrange("b (t p) d -> b p t d", p=P)
        out_b = out.rearrange("b (t p) d -> b p t d", p=P)

        STACK_DMAS = QUAD * 6


        def way_in(tile, later=()):
            return [("qk", tile, which, c) for which in range(2) for c in range(NC)]

        def schedule(prev, nxt):
            at = [[] for _ in range(TOTAL + 2)]
            at[0] += [("v", 0), ("v", 1)]
            at[3] += [("v", 2)]
            at[4] += [("v", 3)]
            for g in range(NQ):
                if g < NQ - 1 or nxt:
                    at[NS * g + SPREAD] += [("m", g)]
                at[NS * g + 6] += [("o", g, 0)]
                at[min(NS * (g + 1) + 1, TOTAL)] += [("o", g, 1)]
            if prev:
                at[1] += [("attT", 0, 0), ("attT", 0, 1)]
                at[2] += [("attT", 1, 0), ("attT", 1, 1)]
                for w in range(4):
                    at[4 + w] += [("wo", w)]
                slot = 12
                for c in range(NC):
                    for job in ffn(c):
                        at[slot] += [job]
                        slot += 1
            if nxt:
                for n, job in enumerate([("xT", c, kt) for c in range(NC) for kt in range(KD)]):
                    at[8 + n] += [job]
                for n, job in enumerate(way_in(0)):
                    at[12 + n] += [job]
                for n, job in enumerate(way_in(1)):
                    at[27 + 2 * n] += [job]
            return at

        def ffn(c):
            return ([("x2T", c, kt) for kt in range(KD)] + [("low", c)]
                    + [("hid", c, f) for f in range(NF)] + [("back", c), ("res", c, 0), ("res", c, 1)])

        def stats_at(prev, nxt):
            t = []
            if nxt:
                t += [(3, 0, 0), (5, 0, 1)]
            if prev:
                t += [(6, 1, 0), (8, 1, 1), (9, 2, 0), (10, 2, 1), (26, 3, 0), (40, 3, 1)]
            return sorted(t)

        def norms_at(prev, nxt):
            t = []
            if nxt:
                t += [(4, 0, 0), (6, 0, 1)]
            if prev:
                t += [(7, 1, 0), (8, 1, 1), (10, 2, 0), (11, 2, 1), (27, 3, 0), (41, 3, 1)]
            return sorted(t)

        def number(at):
            return {job: n for n, job in enumerate(j for jobs in at for j in jobs)}

        def block(b, prev, main, nxt, at, stats, norms, units_at):
            place = number(at)
            last = len(at)

            def m_jobs_before(n):
                return sum(1 for j in list(place)[:n] if j[0] == "m")

            def pe_program(pe):
                unit = 0

                def scores_for_max(g, i, j):
                    nonlocal unit
                    if unit >= 2:
                        pe.wait_ge(max_read, unit - 1)
                    r, p = 64 * (j % 2), j // 2
                    keys = (i + 1) * P
                    for k0 in range(0, keys, CH):
                        k1 = min(k0 + CH, keys)
                        mm = nc.tensor.matmul(ps_max[:, unit % 2, k0:k1], qst[r:r + STACK, g, p, i * P:(i + 1) * P],
                                              kst[r:r + STACK, g, p, k0:k1], start=True, stop=True)
                    mm.then_inc(max_full, 1)
                    unit += 1

                def scores(s, j):
                    g, k = divmod(s, NS)
                    c, kt = STEPS[k]
                    q0, n = width(k)
                    u = QUAD * s + j
                    if u >= 2:
                        pe.wait_ge(exp_done, u - 1)
                    r, p = 64 * (j % 2), j // 2
                    nc.tensor.matmul(ps_st[:, u % 2, 0:n], kst[r:r + STACK + 2, g, p, kt * P:(kt + 1) * P],
                                     qst[r:r + STACK + 2, g, p, q0:q0 + n], start=True, stop=True).then_inc(st_full, 1)

                def times_v(s):
                    g, k = divmod(s, NS)
                    c, kt = STEPS[k]
                    q0, n = width(k)
                    pe.wait_ge(exp_done, QUAD * (s + 1))
                    if diagonal(k):
                        pe.wait_ge(masked, diagonals(s + 1))
                    if kt == 0 and NC * g + c >= 1:
                        pe.wait_ge(acc_read, NC * g + c)
                    if g == 0 and kt % 2 == 0:
                        pe.wait_ge(side_free, place[("v", kt // 2)] + 1)
                    for j in range(QUAD):
                        h = QUAD * g + j
                        mm = nc.tensor.matmul(ps_pv[32 * j:32 * j + 32, q0 - c * CH:q0 - c * CH + n],
                                              vaug[:, kt, h * VW:h * VW + 32], prob[:, s % RING, j, 0:n],
                                              start=(kt == 0), stop=(kt == TC * (c + 1) - 1))
                    mm.then_inc(pv_done, 1)

                def job(what, *a):
                    n = place[(what, *a)]
                    if n:
                        pe.wait_ge(side_free, n)
                    mm = None
                    if what in ("xT", "attT", "x2T"):
                        c, kt = a
                        if what == "attT":
                            src, t0 = att, TC * c
                        else:
                            src, t0 = (xin if what == "xT" else y), TC * c
                            pe.wait_ge(norm_done[0 if what == "xT" else 2], c + 1)
                        for t in range(TC):
                            mm = nc.tensor.transpose(ps_side[:, t * P:(t + 1) * P],
                                                     src[:, t0 + t, kt * P:(kt + 1) * P], ident[:, :])
                    elif what == "qk":
                        tile, which, c = a
                        col = which * D + tile * P
                        for kt in range(KD):
                            mm = nc.tensor.matmul(ps_side[:, :], wqkv[:, kt, col:col + P],
                                                  xnT[:, kt, c * CH:(c + 1) * CH], start=(kt == 0), stop=(kt == KD - 1))
                    elif what in ("v", "wo"):
                        w, = a
                        src, wt, col = (xnT, wqkv, 2 * D) if what == "v" else (attT, wo, 0)
                        for t in range(2):
                            for kt in range(KD):
                                t0 = (2 * w + t) * P
                                mm = nc.tensor.matmul(ps_side[:, t * D:(t + 1) * D], src[:, kt, t0:t0 + P],
                                                      wt[:, kt, col:col + D], start=(kt == 0), stop=(kt == KD - 1))
                    elif what == "m":
                        pe.wait_ge(max_read, NU * (m_jobs_before(n) + 1))
                        mm = nc.tensor.transpose(ps_side[0:QUAD * NT, 0:P], rmax[:, :], ident[:, :])
                    elif what == "o":
                        g, c = a
                        pe.wait_ge(acc_read, NC * g + c + 1)
                        for t in range(TC):
                            mm = nc.tensor.transpose(ps_side[:, t * P:(t + 1) * P],
                                                     oacc[:, c, t * P:(t + 1) * P], ident[:, :])
                    elif what == "low":
                        c, = a
                        for kt in range(KD):
                            mm = nc.tensor.matmul(ps_side[0:RANK, :], u1s[:, kt, :], x2T[:, kt, :],
                                                  start=(kt == 0), stop=(kt == KD - 1))
                    elif what == "hid":
                        c, f = a
                        mm = nc.tensor.matmul(ps_side[:, :], v1s[:, f * P:(f + 1) * P], lowT[:, :], start=True, stop=True)
                    elif what == "back":
                        c, = a
                        pe.wait_ge(gelu_done, c + 1)
                        for f in range(NF):
                            r = RANK * (f % 2)
                            mm = nc.tensor.matmul(ps_side[r:r + RANK, :], u2s[:, f, :], hid[:, f, :],
                                                  start=(f < 2), stop=(f >= NF - 2))
                    elif what == "res":
                        c, w = a
                        for t in range(2):
                            t0 = (2 * w + t) * P
                            mm = nc.tensor.matmul(ps_side[:, t * D:(t + 1) * D], backT[:, t0:t0 + P], v2s[:, :],
                                                  start=True, stop=True)
                    mm.then_inc(side_full, 1)

                for s in range(last):
                    if main and s < TOTAL:
                        g, k = divmod(s, NS)
                        units = units_at[s]
                        g_next = (g + 1) % NQ
                        if k == 0 and units:
                            if g_next in (0, NQ - 1):
                                pe.wait_ge(stacked[g_next], 16 * STACK_DMAS)
                        if k == 0 and g >= 1:
                            pe.wait_ge(mrow_set, 16 * MROW_DMAS * g)
                        done = 0
                        for j in range(QUAD):
                            scores(s, j)
                            upto = len(units) * (j + 1) // QUAD
                            for i, jj in units[done:upto]:
                                scores_for_max(g_next, i, jj)
                            done = upto
                        if s >= 1:
                            times_v(s - 1)
                    elif main and s == TOTAL:
                        times_v(TOTAL - 1)
                    elif not main:
                        if units_at[s]:
                            pe.wait_ge(stacked[0], 16 * STACK_DMAS)
                        for i, jj in units_at[s]:
                            scores_for_max(0, i, jj)
                    for j in at[s]:
                        job(*j)

            def act_program(act):
                highs = 0

                def exponentials(s):
                    g, k = divmod(s, NS)
                    _, n = width(k)
                    if s >= RING:
                        act.wait_ge(pv_done, s - RING + 1)
                    for j in range(QUAD):
                        u = QUAD * s + j
                        act.wait_ge(st_full, u + 1)
                        nc.scalar.activation(prob[:, s % RING, j, 0:n], ps_st[:, u % 2, 0:n], ACT.Exp,
                                             scale=float(DK) ** -0.5).then_inc(exp_done, 1)

                def outputs(s):
                    g, k = divmod(s, NS)
                    c, kt = STEPS[k]
                    if kt != TC * (c + 1) - 1:
                        return
                    act.wait_ge(pv_done, s + 1)
                    if g:
                        act.wait_ge(side_full, place[("o", g - 1, c)] + 1)
                    nc.scalar.activation(oacc[:, c, :], ps_pv[:, :], ACT.Copy).then_inc(acc_read, 1)

                def job(what, *a):
                    nonlocal highs
                    n = place[(what, *a)]
                    if what in ("o", "res"):
                        return
                    act.wait_ge(side_full, n + 1)
                    if what in ("xT", "attT", "x2T"):
                        c, kt = a
                        dst = {"xT": xnT, "attT": attT, "x2T": x2T}[what]
                        c0 = 0 if what == "x2T" else c * CH
                        nc.scalar.activation(dst[:, kt, c0:c0 + CH], ps_side[:, :], ACT.Copy).then_inc(side_free, 1)
                    elif what == "qk":
                        tile, which, c = a
                        if (which, c) == (0, 0) and (tile or main):
                            act.wait_ge(stacked[1 if tile else NQ - 1], 16 * STACK_DMAS)
                        nc.scalar.activation(parts[:, which, 0, c * CH:(c + 1) * CH], ps_side[:, :],
                                             ACT.Copy).then_inc(high_done, 1)
                        highs += 1
                    elif what == "v":
                        w, = a
                        nc.scalar.activation(
                            vaug[:, 2 * w:2 * w + 2, 0:H * VW].rearrange("p t (h e) -> p t h e", e=VW)[:, :, :, 0:DK],
                            ps_side[:, :].rearrange("p (t h e) -> p t h e", t=2, e=DK), ACT.Copy).then_inc(side_free, 1)
                    elif what == "wo":
                        w, = a
                        nc.scalar.activation(y[:, 2 * w:2 * w + 2, :].rearrange("p t d -> p (t d)"), ps_side[:, :],
                                             ACT.Copy).then_inc(side_free, 1)
                    elif what == "m":
                        before = m_jobs_before(n)
                        if before:
                            act.wait_ge(mrow_set, 16 * MROW_DMAS * before)
                        nc.scalar.activation(mrow[:, 0, :], ps_side[0:QUAD * NT, 0:P], ACT.Copy,
                                             scale=-1.0).then_inc(high_done, 1)
                        highs += 1
                    elif what == "low":
                        nc.scalar.activation(lowT[:, :], ps_side[0:RANK, :], ACT.Copy).then_inc(side_free, 1)
                    elif what == "hid":
                        c, f = a
                        nc.scalar.activation(hid[:, f, :], ps_side[:, :], ACT.Identity,
                                             bias=b1s[:, f:f + 1]).then_inc(side_free, 1)
                        if f == NF - 1:
                            act.wait_ge(side_free, n + 1)
                            flat = hid[:, :, :].rearrange("p f n -> p (f n)")
                            nc.scalar.activation(flat, flat, ACT.Gelu_apprx_tanh).then_inc(gelu_done, 1)
                    elif what == "back":
                        nc.scalar.activation(backT[:, :], ps_side[:, :], ACT.Copy).then_inc(side_free, 1)

                for s in range(last):
                    if main and s < TOTAL:
                        exponentials(s)
                        if s >= 1:
                            outputs(s - 1)
                    elif main and s == TOTAL:
                        outputs(TOTAL - 1)
                    for j in at[s]:
                        job(*j)

            def dve_program(dve):
                unit = 0
                steps = 0
                highs = 0

                def step(ins):
                    nonlocal steps
                    steps += 1
                    ins.then_inc(dve_step, 1)
                    return steps

                def maxima(i, j):
                    nonlocal unit
                    dve.wait_ge(max_full, unit + 1)
                    keys = (i + 1) * P
                    nc.vector.tensor_tensor_reduce(
                        out=ps_max[:, unit % 2, 0:keys], in0=ps_max[:, unit % 2, 0:keys], in1=mask[:, S - keys:S], scale=1.0,
                        scalar=NEG, op0=ALU.add, op1=ALU.max,
                        accum_out=rmax[:, j * NT + i:j * NT + i + 1]).then_inc(max_read, 1)
                    unit += 1

                def statistics(n, c):
                    if n == 0:
                        dve.wait_ge(xin_loaded[c], 16)
                        src = xin
                    elif n == 1:
                        dve.wait_ge(side_free, place[("wo", 2 * c + 1)] + 1)
                        src = y
                    elif n == 2:
                        dve.wait_ge(norm_done[1], c + 1)
                        src = xres
                    else:
                        dve.wait_ge(side_free, place[("res", c, 1)] + 1)
                        src = y
                    if c:
                        dve.wait_ge(norm_done[n], c)
                    for t in range(TC):
                        at_ = step(nc.vector.bn_stats(bst[:, n, t, :], src[:, TC * c + t, :]))
                    dve.wait_ge(dve_step, at_)
                    for t in range(TC):
                        ins = nc.vector.bn_aggr(mv[:, n, t, :], bst[:, n, t, :])
                        if t < TC - 1:
                            step(ins)
                    ins.then_inc(stats_done[n], 1)

                def job(what, *a):
                    nonlocal highs
                    n = place[(what, *a)]
                    if what == "qk":
                        tile, which, c = a
                        highs += 1
                        dve.wait_ge(high_done, highs)
                        nc.vector.tensor_tensor(parts[:, which, 1, c * CH:(c + 1) * CH], ps_side[:, :],
                                                parts[:, which, 0, c * CH:(c + 1) * CH].bitcast(F32),
                                                ALU.subtract).then_inc(side_free, 1)
                    elif what == "m":
                        highs += 1
                        dve.wait_ge(high_done, highs)
                        nc.vector.scalar_tensor_tensor(
                            out=mrow[:, 1, :], in0=ps_side[0:QUAD * NT, 0:P], scalar=-1.0,
                            in1=mrow[:, 0, :].bitcast(F32), op0=ALU.mult, op1=ALU.subtract).then_inc(side_free, 1)
                    elif what == "o":
                        g, c = a
                        dve.wait_ge(side_full, n + 1)
                        tiles = ps_side[:, :].rearrange("p (t j e) -> p t j e", t=TC, e=32)
                        at_ = step(nc.vector.reciprocal(rden[:, :, :], tiles[:, :, :, DK]))
                        dve.wait_ge(dve_step, at_)
                        nc.vector.tensor_tensor(
                            att[:, TC * c:TC * (c + 1), g * QUAD * DK:(g + 1) * QUAD * DK]
                            .rearrange("p t (j e) -> p t j e", e=DK),
                            tiles[:, :, :, 0:DK], rden[:, :, :].unsqueeze(3).to_broadcast([P, TC, QUAD, DK]),
                            ALU.mult).then_inc(side_free, 1)
                    elif what == "res":
                        c, w = a
                        dve.wait_ge(side_full, n + 1)
                        t0 = TC * c + 2 * w
                        nc.vector.tensor_tensor(y[:, t0:t0 + 2, :], ps_side[:, :].rearrange("p (t d) -> p t d", t=2),
                                                b2s[:, :].unsqueeze(1).to_broadcast([P, 2, D]),
                                                ALU.add).then_inc(side_free, 1)

                for s in range(last):
                    if s < len(units_at):
                        for i, j in units_at[s]:
                            maxima(i, j)
                    for j in at[s]:
                        job(*j)
                    for when, n, c in stats:
                        if when == s:
                            statistics(n, c)

            def pool_program(pool):
                steps = 0

                def step(ins):
                    nonlocal steps
                    steps += 1
                    ins.then_inc(pool_step, 1)
                    return steps

                def mask_diagonal(s):
                    pool.wait_ge(exp_done, QUAD * (s + 1))
                    tile = prob[:, s % RING, :, 0:P]
                    nc.gpsimd.affine_select(out=tile, in_=tile, compare_op=ALU.is_ge, fill=0.0, base=0,
                                            pattern=[[0, QUAD], [1, P]], channel_multiplier=-1).then_inc(masked, 1)

                def normalise(n, c):
                    pool.wait_ge(stats_done[n], c + 1)
                    var = mv[:, n, :, 1]
                    k = step(nc.gpsimd.tensor_scalar(rstd[:, n, :], var, EPS, None, ALU.add))
                    pool.wait_ge(pool_step, k)
                    k = step(nc.gpsimd.tensor_tensor(out=rstd[:, n, :], in0=rstd[:, n, :], in1=mhalf[:, 0:TC], op=ALU.pow))
                    pool.wait_ge(pool_step, k)
                    if n == 1 and c == 0:
                        pool.wait_ge(xres_loaded, 16)
                    if n == 3:
                        pass
                    for t in range(TC):
                        tt = TC * c + t
                        src = {0: xin, 1: y, 2: xres, 3: y}[n]
                        dst = {0: xin, 1: y, 2: y, 3: y}[n]
                        ins = nc.gpsimd.tensor_scalar(dst[:, tt, :], src[:, tt, :], mv[:, n, t, 0:1],
                                                      rstd[:, n, t:t + 1], ALU.subtract, ALU.mult)
                        if n in (0, 2):
                            if t < TC - 1:
                                step(ins)
                        else:
                            k = step(ins)
                    if n in (1, 3):
                        pool.wait_ge(pool_step, k)
                        dst = xres if n == 1 else y
                        sl = slice(TC * c, TC * (c + 1))
                        ins = nc.gpsimd.tensor_tensor(out=dst[:, sl, :], in0=y[:, sl, :], in1=xres[:, sl, :], op=ALU.add)
                    ins.then_inc(norm_done[n], 1)

                for s in range(last):
                    if main and s < TOTAL and diagonal(s % NS):
                        mask_diagonal(s)
                    for when, n, c in norms:
                        if when == s:
                            normalise(n, c)

            def stack(sp, g):
                for j in range(QUAD):
                    src0 = (QUAD * (g % 2) + j) * DK
                    r, p = 64 * (j % 2), j // 2
                    for dst, which, order in ((qst, 0, (0, 1, 0)), (kst, 1, (0, 0, 1))):
                        for n, part in enumerate(order):
                            sp.dma_start(dst[r + n * DK:r + (n + 1) * DK, g, p, :].bitcast(F32),
                                         parts[src0:src0 + DK, which, part, :].bitcast(F32)).then_inc(stacked[g], 16)

            def max_rows(sp, g, count):
                sp.wait_ge(side_free, place[("m", g)] + 1)
                gn = (g + 1) % NQ
                for j in range(QUAD):
                    r, p = 64 * (j % 2) + STACK, j // 2
                    for part in range(2):
                        sp.dma_start(qst[r + part:r + part + 1, gn, p, :].bitcast(F32).rearrange("a (i q) -> a i q", q=P),
                                     mrow[NT * j:NT * (j + 1), part, :].bitcast(F32)).then_inc(mrow_set, 16)

            def sp_program(sp):
                if prev:
                    sp.dma_start(xres[:, :, :], x_b[bass.ds(b - 1, 1)][0] if not isinstance(b, int) else x_b[b - 1])\
                      .then_inc(xres_loaded, 16)
                if nxt:
                    bn = b + 1
                    for c in range(NC):
                        sl = slice(TC * c, TC * (c + 1))
                        src = x_b[bn] if isinstance(bn, int) else x_b[bass.ds(bn, 1)][0]
                        sp.dma_start(xin[:, sl, :], src[:, sl, :]).then_inc(xin_loaded[c], 16)
                ms = 0
                if main:
                    stack(sp, NQ - 1)
                    for g in range(NQ):
                        if g < NQ - 1 or nxt:
                            max_rows(sp, g, ms)
                            ms += 1
                        if nxt and g < NQ - 1:
                            sp.wait_ge(side_free, place[("qk", g // 2, 1, NC - 1)] + 1)
                            sp.wait_ge(st_full, QUAD * NS * (g + 1))
                            stack(sp, g)
                elif nxt:
                    for g in range(NQ - 1):
                        sp.wait_ge(side_free, place[("qk", g // 2, 1, NC - 1)] + 1)
                        stack(sp, g)
                    max_rows(sp, NQ - 1, ms)
                    ms += 1
                if prev:
                    for c in range(NC):
                        sp.wait_ge(norm_done[3], c + 1)
                        sl = slice(TC * c, TC * (c + 1))
                        dst = out_b[b - 1] if isinstance(b, int) else out_b[bass.ds(b - 1, 1)][0]
                        sp.dma_start(dst[:, sl, :], y[:, sl, :]).then_inc(stored, 16)
                if main:
                    sp.wait_ge(stacked[NQ - 1], 16 * STACK_DMAS)
                if nxt:
                    for g in range(NQ - 1):
                        sp.wait_ge(stacked[g], 16 * STACK_DMAS)
                if ms:
                    sp.wait_ge(mrow_set, 16 * MROW_DMAS * ms)
                if prev:
                    sp.wait_ge(stored, 16 * NC)

            for s_ in sems:
                nc.sync.sem_clear(s_)
            nc.all_engine_barrier()
            with nc.Block() as blk:
                blk.tensor(pe_program)
                blk.scalar(act_program)
                blk.vector(dve_program)
                blk.gpsimd(pool_program)
                blk.sync(sp_program)

        MROW_DMAS = 2 * QUAD

        with nc.Block() as blk:
            @blk.sync
            def _(sp):
                loads = [(wqkv, w_qkv_t.rearrange("(k p) m -> p k m", p=P)), (wo, w_o_t.rearrange("(k p) m -> p k m", p=P)),
                         (u1s, u1.rearrange("(k p) r -> p k r", p=P)), (v1s, v1), (b1s, b1_t),
                         (u2s, u2.rearrange("(f p) r -> p f r", p=P)),
                         (v2s[0:RANK, :], v2), (v2s[RANK:2 * RANK, :], v2),
                         (b2s, b2.partition_broadcast(P)), (ident, ident_in)]
                for dst, src in loads:
                    sp.dma_start(dst[:], src).then_inc(w_loaded, 16)
                sp.wait_ge(w_loaded, 16 * len(loads))

            @blk.vector
            def _(dve):
                nc.vector.memset(mhalf[:, :], -0.5)
                for r in (32, 96):
                    nc.vector.memset(kst[r:r + 32, :, :, :].bitcast(F32), 1.0)
                    nc.vector.memset(qst[r:r + 32, :, :, :].bitcast(F32), 0.0)
                nc.vector.memset(vaug[:, :, H * VW:], 0.0)
                nc.vector.memset(vaug[:, :, 0:H * VW].rearrange("p t (h e) -> p t h e", e=VW)[:, :, :, DK], 1.0)

            @blk.gpsimd
            def _(pool):
                nc.gpsimd.memset(mask[:, :], 0.0).then_inc(consts_set, 1)
                pool.wait_ge(consts_set, 1)
                tri = mask[:, S - P:S]
                nc.gpsimd.affine_select(out=tri, in_=tri, compare_op=ALU.is_ge, fill=NEG, base=0,
                                        pattern=[[-1, P]], channel_multiplier=1)

        at = [[("xT", c, kt) for c in range(NC) for kt in range(KD)], way_in(0), way_in(1), [], [("m", NQ - 1)]]
        units = [[], [], [], UNITS, []]
        block(-1, False, False, True, at, [(0, 0, 0), (0, 0, 1)], [(0, 0, 0), (0, 0, 1)], units)

        def full(b, prev, nxt):
            units_at = []
            for s in range(TOTAL):
                g, k = divmod(s, NS)
                units_at.append(UNITS_AT[k] if g < NQ - 1 or nxt else [])
            block(b, prev, True, nxt, schedule(prev, nxt), stats_at(prev, nxt), norms_at(prev, nxt), units_at)

        full(0, False, True)
        with nc.Fori(1, B - 1) as b:
            full(b, True, True)
        full(B - 1, True, False)

        at = [[("attT", c, kt) for c in range(NC) for kt in range(KD)] + [("wo", w) for w in range(4)]]
        at += [ffn(0), [], ffn(1), []]
        block(B, True, False, False, at,
              [(0, 1, 0), (0, 1, 1), (0, 2, 0), (0, 2, 1), (2, 3, 0), (4, 3, 1)],
              [(0, 1, 0), (0, 1, 1), (0, 2, 0), (0, 2, 1), (2, 3, 0), (4, 3, 1)], [[] for _ in at])


def kernel(L0_attn_x, L0_attn_w_qkv, L0_attn_w_o, L0_ffn_U1, L0_ffn_V1, L0_ffn_b1, L0_ffn_U2, L0_ffn_V2, L0_ffn_b2):
    import numpy as np
    from concourse import bacc
    from concourse.bass_utils import run_bass_kernel_spmd

    x = np.ascontiguousarray(L0_attn_x)
    d = x.shape[-1]
    arrays = {
        "x": x,
        "w_qkv_t": np.ascontiguousarray(np.asarray(L0_attn_w_qkv).reshape(3 * d, d).T),
        "w_o_t": np.ascontiguousarray(np.asarray(L0_attn_w_o).T),
        "u1": np.ascontiguousarray(L0_ffn_U1),
        "v1": np.ascontiguousarray(L0_ffn_V1),
        "b1_t": np.ascontiguousarray(np.asarray(L0_ffn_b1).reshape(-1, P).T),
        "u2": np.ascontiguousarray(L0_ffn_U2),
        "v2": np.ascontiguousarray(L0_ffn_V2),
        "b2": np.ascontiguousarray(L0_ffn_b2),
        "ident_in": np.eye(P, dtype=np.float32),
    }
    nc = bacc.Bacc("TRN2", target_bir_lowering=False, num_devices=1)
    args = [nc.dram_tensor(n + "_dram", list(a.shape), mybir.dt.from_np(a.dtype), kind="ExternalInput").ap()
            for n, a in arrays.items()]
    out = nc.dram_tensor("out_dram", list(x.shape), F32, kind="ExternalOutput").ap()
    build(nc, *args, out)
    return run_bass_kernel_spmd(nc, [{n + "_dram": a for n, a in arrays.items()}], core_ids=[0]).results[0]["out_dram"]
```
